# Optimizing a Trainium2 kernel written in Bass

```python
import numpy as np
import jax
import jax.numpy as jnp

def _softmax(x, axis=-1):
    return jax.nn.softmax(x, axis=axis)

def _gelu(x):
    return jax.nn.gelu(x, approximate=True)

def _silu(x):
    return jax.nn.silu(x)

def _sigmoid(x):
    return jax.nn.sigmoid(x)

def _layernorm(x, axis=-1, eps=1e-05):
    m = jnp.mean(x, axis=axis, keepdims=True)
    v = jnp.var(x, axis=axis, keepdims=True)
    return (x - m) / jnp.sqrt(v + eps)

def _scatter_add(tgt, idx, src, axis=0):
    return tgt.at[idx].add(src)

def _segment_sum(src, seg, n):
    return jax.ops.segment_sum(src, seg, n)
kernel_name = 'mk_rec_standalone_d1_rec_r8_52ae2d'

def setup_inputs(seed: int=0):
    np.random.seed(seed)
    _w = jnp.asarray

    def _rec_inputs():
        import jax
        import jax.numpy as jnp
        _rk = jax.random.key(seed)
        r_inputs_A = -0.000292821 + 1.00034 * jax.random.normal(jax.random.fold_in(_rk, 1), (512, 32, 64), jnp.float32)
        r_inputs_B = -1.39393e-06 + 0.999914 * jax.random.normal(jax.random.fold_in(_rk, 2), (512, 32, 64), jnp.float32)
        return (r_inputs_A, r_inputs_B)
    r_inputs_A, r_inputs_B = _rec_inputs()

    def _L0_rec_setup():
        import jax, jax.numpy as jnp
        import numpy as np
        BATCH, F, E = (256, 32, 64)
        key = jax.random.key(seed)
        kA, kB, kW = jax.random.split(key, 3)
        inputs_A = jax.random.normal(kA, (BATCH, F, E), dtype=jnp.float32)
        inputs_B = jax.random.normal(kB, (BATCH, F, E), dtype=jnp.float32)
        W = jax.random.normal(kW, (F, E, E), dtype=jnp.float32) * (1.0 / np.sqrt(E))
        return {'inputs_A': inputs_A, 'inputs_B': inputs_B, 'W': W}
    _L0_rec_all = _L0_rec_setup()
    _L0_rec_in = {k: v for k, v in _L0_rec_all.items() if k in ('W',)}
    del _L0_rec_all
    return {'r_inputs_A': r_inputs_A, 'r_inputs_B': r_inputs_B, 'L0_rec_W': _L0_rec_in['W']}

def reference(r_inputs_A, r_inputs_B, L0_rec_W):
    import jax
    import jax.numpy as jnp

    def _L0_rec_ref(inputs_A, inputs_B, W):
        import jax, jax.numpy as jnp
        import numpy as np
        BATCH, F, E = (256, 32, 64)
        proj = jnp.einsum('bfe,fde->bfd', inputs_A, W)
        B_, F_, E_ = inputs_A.shape
        p = proj[:, :, None, :] * inputs_B[:, None, :, :]
        return p.reshape(B_, F_ * F_, E_)
    y = _L0_rec_ref(r_inputs_A, r_inputs_B, L0_rec_W)
    return y

_drawn_inputs = setup_inputs


def setup_inputs(seed=0):
    import zlib

    import numpy as np

    out = dict(_drawn_inputs(seed))
    spreads = {}
    factors = {}
    for name, (base, spread) in spreads.items():
        noise = np.random.default_rng([zlib.crc32(name.encode()), seed]).standard_normal(out[name].shape)
        drawn = base * np.exp(spread * noise) if base else spread * noise
        out[name] = jnp.asarray(drawn.astype(out[name].dtype))
    for name, factor in factors.items():
        out[name] = (out[name] * factor).astype(out[name].dtype)
    return out
```

```python
from contextlib import ExitStack

import concourse.bass as bass
from concourse import mybir

F32 = mybir.dt.float32
ALU = mybir.AluOpType
ACT = mybir.ActivationFunctionType


def projected_pairwise_products(nc: bass.Bass, A: bass.AP, B: bass.AP, W: bass.AP, out: bass.AP):
    BATCH, F, E = A.shape
    P = 128
    TILES = BATCH // P
    GF = 512 // E
    GROUPS = F // GF
    CF = 2
    CPG = GF // CF
    CHUNKS = F // CF
    SLOTS = 8
    ROUNDS = CHUNKS // SLOTS
    WC = F * E // P
    WPG = WC // GROUPS
    H = P // E

    A_rows = A.rearrange("(t p) f e -> t p (f e)", p=P)
    B_rows = B.rearrange("(t p) f e -> p t (f e)", p=P)
    W_rows = W.rearrange("f d e -> (f d) e").rearrange("(c p) e -> p c e", p=P)
    out_rows = out.rearrange("b r e -> b (r e)")
    CHUNK = CF * F * E

    with ExitStack() as ctx:
        def sb(name, shape):
            return ctx.enter_context(nc.sbuf_tensor(name, shape, F32))

        def sem(name):
            return ctx.enter_context(nc.semaphore(name))

        a_sb = sb("a_sb", [P, F * E])
        b_sb = sb("b_sb", [P, TILES, F * E])
        w_sb = sb("w_sb", [P, WC, E])
        wT = sb("wT", [E, WC // H, H, P])
        aT = sb("aT", [E, 2, GF // H, H, P])
        ident = sb("ident", [P, P])
        ring = sb("ring", [P, SLOTS, CHUNK])
        ps_aT = ctx.enter_context(nc.psum_tensor("ps_aT", [P, 2, GF // H, P], F32))
        ps_wT = ctx.enter_context(nc.psum_tensor("ps_wT", [P, 2, GF // H, P], F32))
        ps_proj = ctx.enter_context(nc.psum_tensor("ps_proj", [P, GROUPS, GF * E], F32))

        ident_zeroed = sem("ident_zeroed")
        ident_ready = sem("ident_ready")
        w_loaded = sem("w_loaded")
        a_loaded = sem("a_loaded")
        b_first_loaded = sem("b_first_loaded")
        b_rest_loaded = sem("b_rest_loaded")
        wT_in_psum = sem("wT_in_psum")
        wT_copied = sem("wT_copied")
        aT_in_psum = sem("aT_in_psum")
        aT_copied = sem("aT_copied")
        proj_ready = sem("proj_ready")
        products_ready = sem("products_ready")
        stored = [sem(f"stored{s}") for s in range(SLOTS)]

        block = ctx.enter_context(nc.Block())

        @block.gpsimd
        def _(pool):
            nc.gpsimd.memset(ident[:], 0.0).then_inc(ident_zeroed, 1)
            pool.wait_ge(ident_zeroed, 1)
            nc.gpsimd.affine_select(out=ident[:], in_=ident[:], compare_op=ALU.not_equal, fill=1.0, base=0,
                                    pattern=[[-1, P]], channel_multiplier=1).then_inc(ident_ready, 1)

        @block.sync
        def _(sp):
            sp.dma_start(w_sb[:], W_rows).then_inc(w_loaded, 16)
            sp.dma_start(b_sb[:, 0, :], B_rows[:, 0, :]).then_inc(b_first_loaded, 16)
            sp.dma_start(b_sb[:, 1:TILES, :], B_rows[:, 1:TILES, :]).then_inc(b_rest_loaded, 16)
            with sp.Fori(0, TILES) as t:
                for c in range(CHUNKS):
                    s = c % SLOTS
                    sp.wait_ge(products_ready, t * CHUNKS + c + 1)
                    sp.dma_start(out_rows[bass.ds(t * P, P), c * CHUNK:(c + 1) * CHUNK],
                                 ring[:, s, :]).then_inc(stored[s], 16)
            for s in range(SLOTS):
                sp.wait_ge(stored[s], 16 * TILES * ROUNDS)

        @block.scalar
        def _(act):
            def copy_aT(n, q):
                act.wait_ge(aT_in_psum, n + 1)
                if not (isinstance(n, int) and n < 2):
                    act.wait_ge(proj_ready, n - 1)
                for h in range(H):
                    last = nc.scalar.activation(aT[:, q % 2, :, h, :], ps_aT[h * E:(h + 1) * E, q % 2, :, :], ACT.Copy)
                last.then_inc(aT_copied, 1)

            act.dma_start(a_sb[:], A_rows[0]).then_inc(a_loaded, 16)
            for q in range(GROUPS):
                act.wait_ge(wT_in_psum, q + 1)
                for h in range(H):
                    last = nc.scalar.activation(wT[:, q * WPG // H:(q + 1) * WPG // H, h, :],
                                                ps_wT[h * E:(h + 1) * E, q % 2, 0:WPG // H, :], ACT.Copy)
                last.then_inc(wT_copied, 1)
                copy_aT(q, q)
            with act.Fori(1, TILES) as t:
                act.wait_ge(aT_in_psum, t * GROUPS)
                act.dma_start(a_sb[:], A_rows[bass.ds(t, 1)].rearrange("o p x -> (o p) x")).then_inc(a_loaded, 16)
                for q in range(GROUPS):
                    copy_aT(t * GROUPS + q, q)

        @block.tensor
        def _(pe):
            wT_cols = wT[:].rearrange("e c h r -> e (c h r)")

            def turn_W(q):
                if q >= 2:
                    pe.wait_ge(wT_copied, q - 1)
                for j in range(WPG // H):
                    c = q * WPG + j * H
                    last = nc.tensor.transpose(ps_wT[:, q % 2, j, :],
                                               w_sb[:, c:c + H, :].rearrange("p c e -> p (c e)"), ident[:])
                last.then_inc(wT_in_psum, 1)

            def turn_A(n, q):
                if not (isinstance(n, int) and n < 2):
                    pe.wait_ge(aT_copied, n - 1)
                for j in range(GF // H):
                    f = q * GF + j * H
                    last = nc.tensor.transpose(ps_aT[:, q % 2, j, :], a_sb[:, f * E:(f + H) * E], ident[:])
                last.then_inc(aT_in_psum, 1)

            def project(n, q):
                pe.wait_ge(aT_copied, n + 1)
                for j in range(GF):
                    f = q * GF + j
                    last = nc.tensor.matmul(ps_proj[:, q, j * E:(j + 1) * E], aT[:, q % 2, j // H, j % H, :],
                                            wT_cols[:, f * E:(f + 1) * E], start=True, stop=True)
                last.then_inc(proj_ready, 1)

            pe.wait_ge(w_loaded, 16)
            pe.wait_ge(ident_ready, 1)
            for q in range(GROUPS):
                turn_W(q)
                if q == 0:
                    pe.wait_ge(a_loaded, 16)
                turn_A(q, q)
                pe.wait_ge(wT_copied, q + 1)
                project(q, q)
            with pe.Fori(1, TILES) as t:
                pe.wait_ge(a_loaded, 16 * t + 16)
                for q in range(GROUPS):
                    turn_A(t * GROUPS + q, q)
                    pe.wait_ge(products_ready, (t - 1) * CHUNKS + (q + 1) * CPG)
                    project(t * GROUPS + q, q)

        @block.vector
        def _(dve):
            def multiply(t, c, reused):
                s, q, j = c % SLOTS, c // CPG, c % CPG
                if j == 0:
                    dve.wait_ge(proj_ready, t * GROUPS + q + 1)
                if reused:
                    dve.wait_ge(stored[s], (t * ROUNDS + c // SLOTS) * 16)
                proj = ps_proj[:, q, j * CF * E:(j + 1) * CF * E].rearrange("p (f o e) -> p f o e", f=CF, o=1)
                b = b_sb[:, bass.ds(t, 1), :].rearrange("p o (g e) -> p o g e", g=F)
                nc.vector.tensor_tensor(ring[:, s, :].rearrange("p (f g e) -> p f g e", f=CF, g=F),
                                        proj.to_broadcast([P, CF, F, E]), b.to_broadcast([P, CF, F, E]),
                                        ALU.mult).then_inc(products_ready, 1)

            dve.wait_ge(b_first_loaded, 16)
            for c in range(CHUNKS):
                multiply(0, c, c >= SLOTS)
            dve.wait_ge(b_rest_loaded, 16)
            with dve.Fori(1, TILES) as t:
                for c in range(CHUNKS):
                    multiply(t, c, True)


def kernel(r_inputs_A, r_inputs_B, L0_rec_W):
    import numpy as np
    import concourse.bacc as bacc
    from concourse.bass_utils import run_bass_kernel_spmd

    nc = bacc.Bacc("TRN2", target_bir_lowering=False, num_devices=1)
    arrays, args = {}, []
    for name, a in (("A", r_inputs_A), ("B", r_inputs_B), ("W", L0_rec_W)):
        arrays[name] = np.ascontiguousarray(a)
        args.append(nc.dram_tensor(name, arrays[name].shape, F32, kind="ExternalInput").ap())
    batch, features, width = arrays["A"].shape
    args.append(nc.dram_tensor("products", (batch, features * features, width), F32, kind="ExternalOutput").ap())
    projected_pairwise_products(nc, *args)
    return run_bass_kernel_spmd(nc, [arrays], core_ids=[0]).results[0]["products"]
```

```python
from contextlib import ExitStack

import concourse.bass as bass
from concourse import mybir

F32 = mybir.dt.float32
ALU = mybir.AluOpType
ACT = mybir.ActivationFunctionType


def projected_pairwise_products(nc: bass.Bass, A: bass.AP, B: bass.AP, W: bass.AP, out: bass.AP):
    BATCH, F, E = A.shape
    P = 128
    TILES = BATCH // P
    GF = 512 // E
    GROUPS = F // GF
    CF = 2
    CPG = GF // CF
    CHUNKS = F // CF
    SLOTS = 8
    ROUNDS = CHUNKS // SLOTS
    WR = GF * E // P
    H = P // E

    A_rows = A.rearrange("(t p) f e -> t p (f e)", p=P)
    B_rows = B.rearrange("(t p) f e -> p t (f e)", p=P)
    W_rows = W.rearrange("f d e -> (f d) e").rearrange("(q p r) e -> p q (r e)", p=P, r=WR)
    out_rows = out.rearrange("b r e -> b (r e)")
    CHUNK = CF * F * E

    with ExitStack() as ctx:
        def sb(name, shape):
            return ctx.enter_context(nc.sbuf_tensor(name, shape, F32))

        def sem(name):
            return ctx.enter_context(nc.semaphore(name))

        a_sb = sb("a_sb", [P, F * E])
        b_sb = sb("b_sb", [P, TILES, F * E])
        w_sb = sb("w_sb", [P, GROUPS, WR * E])
        wT = sb("wT", [E, GROUPS, P, WR])
        aT = sb("aT", [E, 2, GF // H, H, P])
        ident = sb("ident", [P, P])
        ring = sb("ring", [P, SLOTS, CHUNK])
        ps_aT = ctx.enter_context(nc.psum_tensor("ps_aT", [P, 2, GF // H, P], F32))
        ps_wT = ctx.enter_context(nc.psum_tensor("ps_wT", [P, 512], F32))
        ps_wT_rows = ps_wT[:, 0:WR // H * P].rearrange("x (m p) -> x m p", p=P)
        ps_proj = ctx.enter_context(nc.psum_tensor("ps_proj", [P, GROUPS, GF * E], F32))

        ident_zeroed = sem("ident_zeroed")
        ident_ready = sem("ident_ready")
        w_first_loaded = sem("w_first_loaded")
        w_rest_loaded = sem("w_rest_loaded")
        a_first_loaded = sem("a_first_loaded")
        a_rest_loaded = sem("a_rest_loaded")
        a_tile_loaded = sem("a_tile_loaded")
        b_first_loaded = sem("b_first_loaded")
        b_rest_loaded = sem("b_rest_loaded")
        wT_in_psum = sem("wT_in_psum")
        wT_copied = sem("wT_copied")
        aT_in_psum = sem("aT_in_psum")
        aT_copied = sem("aT_copied")
        proj_ready = sem("proj_ready")
        products_ready = sem("products_ready")
        stored = [sem(f"stored{s}") for s in range(SLOTS)]

        block = ctx.enter_context(nc.Block())

        @block.gpsimd
        def _(pool):
            nc.gpsimd.memset(ident[:], 0.0).then_inc(ident_zeroed, 1)
            pool.wait_ge(ident_zeroed, 1)
            nc.gpsimd.affine_select(out=ident[:], in_=ident[:], compare_op=ALU.not_equal, fill=1.0, base=0,
                                    pattern=[[-1, P]], channel_multiplier=1).then_inc(ident_ready, 1)

        @block.sync
        def _(sp):
            sp.dma_start(a_sb[:, 0:GF * E], A_rows[0, :, 0:GF * E]).then_inc(a_first_loaded, 16)
            sp.dma_start(b_sb[:, 0, :], B_rows[:, 0, :]).then_inc(b_first_loaded, 16)
            sp.dma_start(w_sb[:, 1:GROUPS, :], W_rows[:, 1:GROUPS, :]).then_inc(w_rest_loaded, 16)
            sp.dma_start(a_sb[:, GF * E:], A_rows[0, :, GF * E:]).then_inc(a_rest_loaded, 16)
            sp.dma_start(b_sb[:, 1:TILES, :], B_rows[:, 1:TILES, :]).then_inc(b_rest_loaded, 16)
            with sp.Fori(0, TILES) as t:
                for c in range(CHUNKS):
                    s = c % SLOTS
                    sp.wait_ge(products_ready, t * CHUNKS + c + 1)
                    sp.dma_start(out_rows[bass.ds(t * P, P), c * CHUNK:(c + 1) * CHUNK],
                                 ring[:, s, :]).then_inc(stored[s], 16)
            for s in range(SLOTS):
                sp.wait_ge(stored[s], 16 * TILES * ROUNDS)

        @block.scalar
        def _(act):
            def copy_aT(n, q, reused):
                act.wait_ge(aT_in_psum, n + 1)
                if reused:
                    act.wait_ge(proj_ready, n - 1)
                for h in range(H):
                    last = nc.scalar.activation(aT[:, q % 2, :, h, :], ps_aT[h * E:(h + 1) * E, q % 2, :, :], ACT.Copy)
                last.then_inc(aT_copied, 1)

            act.dma_start(w_sb[:, 0, :], W_rows[:, 0, :]).then_inc(w_first_loaded, 16)
            for q in range(GROUPS):
                act.wait_ge(wT_in_psum, q + 1)
                for h in range(H):
                    last = nc.scalar.activation(wT[:, q, :, h:WR:H].rearrange("e p m -> e m p"),
                                                ps_wT_rows[h * E:(h + 1) * E, :, :], ACT.Copy)
                last.then_inc(wT_copied, 1)
                copy_aT(q, q, q >= 2)
            with act.Fori(1, TILES) as t:
                act.wait_ge(aT_in_psum, t * GROUPS)
                act.dma_start(a_sb[:], A_rows[bass.ds(t, 1)].rearrange("o p x -> (o p) x")).then_inc(a_tile_loaded, 16)
                for q in range(GROUPS):
                    copy_aT(t * GROUPS + q, q, True)

        @block.tensor
        def _(pe):
            wT_cols = wT[:].rearrange("e q p r -> e (q p r)")

            def turn_W(q):
                if q >= 1:
                    pe.wait_ge(wT_copied, q)
                for m in range(WR // H):
                    last = nc.tensor.transpose(ps_wT_rows[:, m, :], w_sb[:, q, m * P:(m + 1) * P], ident[:])
                last.then_inc(wT_in_psum, 1)

            def turn_A(n, q, reused):
                if reused:
                    pe.wait_ge(aT_copied, n - 1)
                for j in range(GF // H):
                    f = q * GF + j * H
                    last = nc.tensor.transpose(ps_aT[:, q % 2, j, :], a_sb[:, f * E:(f + H) * E], ident[:])
                last.then_inc(aT_in_psum, 1)

            def project(n, q):
                pe.wait_ge(aT_copied, n + 1)
                for j in range(GF):
                    f = q * GF + j
                    last = nc.tensor.matmul(ps_proj[:, q, j * E:(j + 1) * E], aT[:, q % 2, j // H, j % H, :],
                                            wT_cols[:, f * E:(f + 1) * E], start=True, stop=True)
                last.then_inc(proj_ready, 1)

            pe.wait_ge(ident_ready, 1)
            for q in range(GROUPS):
                if q == 0:
                    pe.wait_ge(w_first_loaded, 16)
                if q == 1:
                    pe.wait_ge(w_rest_loaded, 16)
                turn_W(q)
                if q == 0:
                    pe.wait_ge(a_first_loaded, 16)
                if q == 1:
                    pe.wait_ge(a_rest_loaded, 16)
                turn_A(q, q, q >= 2)
                pe.wait_ge(wT_copied, q + 1)
                project(q, q)
            with pe.Fori(1, TILES) as t:
                pe.wait_ge(a_tile_loaded, 16 * t)
                for q in range(GROUPS):
                    turn_A(t * GROUPS + q, q, True)
                    pe.wait_ge(products_ready, (t - 1) * CHUNKS + (q + 1) * CPG)
                    project(t * GROUPS + q, q)

        @block.vector
        def _(dve):
            def multiply(t, c, reused):
                s, q, j = c % SLOTS, c // CPG, c % CPG
                if j == 0:
                    dve.wait_ge(proj_ready, t * GROUPS + q + 1)
                if reused:
                    dve.wait_ge(stored[s], (t * ROUNDS + c // SLOTS) * 16)
                proj = ps_proj[:, q, j * CF * E:(j + 1) * CF * E].rearrange("p (f o e) -> p f o e", f=CF, o=1)
                b = b_sb[:, bass.ds(t, 1), :].rearrange("p o (g e) -> p o g e", g=F)
                nc.vector.tensor_tensor(ring[:, s, :].rearrange("p (f g e) -> p f g e", f=CF, g=F),
                                        proj.to_broadcast([P, CF, F, E]), b.to_broadcast([P, CF, F, E]),
                                        ALU.mult).then_inc(products_ready, 1)

            dve.wait_ge(b_first_loaded, 16)
            for c in range(CHUNKS):
                multiply(0, c, c >= SLOTS)
            dve.wait_ge(b_rest_loaded, 16)
            with dve.Fori(1, TILES) as t:
                for c in range(CHUNKS):
                    multiply(t, c, True)


def kernel(r_inputs_A, r_inputs_B, L0_rec_W):
    import numpy as np
    import concourse.bacc as bacc
    from concourse.bass_utils import run_bass_kernel_spmd

    nc = bacc.Bacc("TRN2", target_bir_lowering=False, num_devices=1)
    arrays, args = {}, []
    for name, a in (("A", r_inputs_A), ("B", r_inputs_B), ("W", L0_rec_W)):
        arrays[name] = np.ascontiguousarray(a)
        args.append(nc.dram_tensor(name, arrays[name].shape, F32, kind="ExternalInput").ap())
    batch, features, width = arrays["A"].shape
    args.append(nc.dram_tensor("products", (batch, features * features, width), F32, kind="ExternalOutput").ap())
    projected_pairwise_products(nc, *args)
    return run_bass_kernel_spmd(nc, [arrays], core_ids=[0]).results[0]["products"]
```
